# Optimizing a Trainium2 kernel written in Bass

```python
import numpy as np
import jax
import jax.numpy as jnp

def _softmax(x, axis=-1):
    return jax.nn.softmax(x, axis=axis)

def _gelu(x):
    return jax.nn.gelu(x, approximate=True)

def _silu(x):
    return jax.nn.silu(x)

def _sigmoid(x):
    return jax.nn.sigmoid(x)

def _layernorm(x, axis=-1, eps=1e-05):
    m = jnp.mean(x, axis=axis, keepdims=True)
    v = jnp.var(x, axis=axis, keepdims=True)
    return (x - m) / jnp.sqrt(v + eps)

def _scatter_add(tgt, idx, src, axis=0):
    return tgt.at[idx].add(src)

def _segment_sum(src, seg, n):
    return jax.ops.segment_sum(src, seg, n)
kernel_name = 'mk_cond_resid_d2_seqx_r2_c5e634'

def setup_inputs(seed: int=0):
    np.random.seed(seed)
    _w = jnp.asarray

    def _rec_inputs():
        import jax
        import jax.numpy as jnp
        _rk = jax.random.key(seed)
        x = -7.109e-05 + 0.9999 * jax.random.normal(jax.random.fold_in(_rk, 1), (128, 128, 1024), jnp.float32)
        _lenS = 128 - jax.random.randint(jax.random.fold_in(_rk, 7), (128,), 0, max(1, 128 // 4) + 1, jnp.int32)
        _lenS2 = 128 - jax.random.randint(jax.random.fold_in(_rk, 8), (128,), 0, max(1, 128 // 4) + 1, jnp.int32)
        itok_B_1_198 = jax.random.randint(jax.random.fold_in(_rk, 11), (128,), 1, 199, jnp.int32)
        itok_B_0_7 = jax.random.randint(jax.random.fold_in(_rk, 12), (128,), 0, 8, jnp.int32)
        fside_8xS_0 = -0.00162727 + 0.0609077 * jax.random.normal(jax.random.fold_in(_rk, 13), (8, 128), jnp.float32)
        return (x, itok_B_1_198, itok_B_0_7, fside_8xS_0)
    x, itok_B_1_198, itok_B_0_7, fside_8xS_0 = _rec_inputs()

    def _L0_cond_setup():
        import jax, jax.numpy as jnp
        import numpy as np
        B, C, T = (128, 128, 1024)
        S, D = (200, 128)
        key = jax.random.key(seed)
        k1, k2, k3 = jax.random.split(key, 3)
        x = jax.random.normal(k1, (B, C, T), dtype=jnp.float32)
        conditions = jax.random.randint(k2, (B,), 0, S, dtype=jnp.int64)
        weights = jax.random.normal(k3, (S, C, D), dtype=jnp.float32) / jnp.sqrt(jnp.float32(C))
        return {'x': x, 'conditions': conditions, 'weights': weights}
    _L0_cond_all = _L0_cond_setup()
    _L0_cond_in = {k: v for k, v in _L0_cond_all.items() if k in ('weights',)}
    del _L0_cond_all

    def _L1_cond_setup():
        import jax, jax.numpy as jnp
        import numpy as np
        B, C, T = (64, 128, 1024)
        D, N = (128, 8)
        key = jax.random.key(seed)
        k_x, k_s, k_w, k_b = jax.random.split(key, 4)
        scale = 1.0 / np.sqrt(C)
        x = jax.random.normal(k_x, (B, C, T), dtype=jnp.float32)
        subjects = jax.random.randint(k_s, (B,), 0, N, dtype=jnp.int64)
        weights = jax.random.normal(k_w, (N, C, D), dtype=jnp.float32) * scale
        bias = jax.random.normal(k_b, (N, D), dtype=jnp.float32) * scale
        return {'x': x, 'subjects': subjects, 'weights': weights, 'bias': bias}
    _L1_cond_all = _L1_cond_setup()
    _L1_cond_in = {k: v for k, v in _L1_cond_all.items() if k in ('weights',)}
    del _L1_cond_all
    return {'x': x, 'itok_B_1_198': itok_B_1_198, 'itok_B_0_7': itok_B_0_7, 'fside_8xS_0': fside_8xS_0, 'L0_cond_weights': _L0_cond_in['weights'], 'L1_cond_weights': _L1_cond_in['weights']}

def reference(x, itok_B_1_198, itok_B_0_7, fside_8xS_0, L0_cond_weights, L1_cond_weights):
    import jax
    import jax.numpy as jnp

    def _L0_cond_ref(x, conditions, weights):
        import jax, jax.numpy as jnp
        import numpy as np
        B, C, T = (128, 128, 1024)
        S, D = (200, 128)
        w = weights[conditions]
        return jnp.einsum('bct,bcd->bdt', x, w)

    def _L1_cond_ref(x, subjects, weights, bias):
        import jax, jax.numpy as jnp
        import numpy as np
        B, C, T = (64, 128, 1024)
        D, N = (128, 8)
        w = weights[subjects]
        b = bias[subjects]
        out = jnp.einsum('bct,bcd->bdt', x, w)
        out = out + b[:, :, None]
        return out
    x = x + _L0_cond_ref(x, itok_B_1_198, L0_cond_weights)
    x = x + _L1_cond_ref(x, itok_B_0_7, L1_cond_weights, fside_8xS_0)
    return x

_drawn_inputs = setup_inputs


def setup_inputs(seed=0):
    import zlib

    import numpy as np

    out = dict(_drawn_inputs(seed))
    spreads = {}
    factors = {}
    for name, (base, spread) in spreads.items():
        noise = np.random.default_rng([zlib.crc32(name.encode()), seed]).standard_normal(out[name].shape)
        drawn = base * np.exp(spread * noise) if base else spread * noise
        out[name] = jnp.asarray(drawn.astype(out[name].dtype))
    for name, factor in factors.items():
        out[name] = (out[name] * factor).astype(out[name].dtype)
    return out
```

```python
from contextlib import ExitStack

import concourse.bass as bass
from concourse import mybir

F32 = mybir.dt.float32
I32 = mybir.dt.int32
ALU = mybir.AluOpType
ACT = mybir.ActivationFunctionType


def conditioned_residual_kernel(nc, x, cond0, cond0_col, cond1, bias_t, w0_t, w1, out):
    B, C, T = x.shape
    N0, _, D = w0_t.shape
    N1 = w1.shape[0]
    assert C == D == 128
    PAIR = 2
    RING = 8
    PAIRS = B // PAIR
    ROUNDS = PAIRS // RING
    LAST = RING - 1
    LEAD = 2
    ROUND_B = RING * PAIR
    HALF = T // 2
    MB = 2
    YB = 2
    assert PAIRS % RING == 0 and HALF <= 512 and RING % MB == 0 and ROUND_B % YB == 0

    x_v = x.rearrange("(n k) c t -> n c k t", k=PAIR)
    out_v = out.rearrange("(n k) c t -> n c k t", k=PAIR)

    with ExitStack() as ctx:
        def sb(name, shape, dt=F32):
            return ctx.enter_context(nc.sbuf_tensor(name, shape, dt))

        def sem(name):
            return ctx.enter_context(nc.semaphore(name))

        xy = sb("xy", [C, RING, PAIR, T])
        w0_home = sb("w0_home", [C, B, D])
        w0_pick = sb("w0_pick", [C, RING, PAIR, D])
        j_all = sb("j_all", [C, N1, D + 1])
        j_pick = sb("j_pick", [C, RING, PAIR, D + 1])
        m_sb = sb("m_sb", [C, RING, PAIR, D])
        w1_sb = sb("w1_sb", [C, N1, D])
        bias_sb = sb("bias_sb", [D, N1])
        eye = sb("eye", [C, D])
        cond0_sb = sb("cond0_sb", [1, B], I32)
        cond1_sb = sb("cond1_sb", [1, B], I32)
        cond0_rows = sb("cond0_rows", [B, B], I32)
        cond0_col_sb = sb("cond0_col_sb", [B, 1], I32)
        cond0_f32 = sb("cond0_f32", [B, 1])
        batch_less_b = sb("batch_less_b", [B, B])
        same = sb("same", [B, B])
        same_batch = sb("same_batch", [B, B])
        home_less_b = sb("home_less_b", [B, 1])
        home_row = sb("home_row", [1, B], I32)
        at_home_row = sb("at_home_row", [1, B], I32)
        y_ps = ctx.enter_context(nc.psum_tensor("y_ps", [D, YB, 2, HALF], F32))
        m_ps = ctx.enter_context(nc.psum_tensor("m_ps", [C, MB, 512], F32))
        home_ps = ctx.enter_context(nc.psum_tensor("home_ps", [1, 512], F32))

        cond0_loaded = sem("cond0_loaded")
        cond1_loaded = sem("cond1_loaded")
        cond0_compared = sem("cond0_compared")
        batch_counted = sem("batch_counted")
        home_step = sem("home_step")
        home_turned = sem("home_turned")
        home_ready = sem("home_ready")
        w1_loaded = sem("w1_loaded")
        bias_loaded = sem("bias_loaded")
        x_loaded = [sem(f"x_loaded{s}") for s in range(RING)]
        w0_loaded = [sem(f"w0_loaded{s}") for s in range(RING)]
        stored = [sem(f"stored{s}") for s in range(RING)]
        last_x_loaded = [sem(f"last_x_loaded{n}") for n in range(2 * PAIR)]
        last_stored = sem("last_stored")
        eye_cleared = sem("eye_cleared")
        eye_ready = sem("eye_ready")
        bias_in_j = sem("bias_in_j")
        j_ready = sem("j_ready")
        picked = sem("picked")
        product_ready = sem("product_ready")
        m_ready = [sem(f"m_ready{s}") for s in range(MB)]
        y_ready = sem("y_ready")
        left_out = [sem(f"left_out{s}") for s in range(YB)]
        right_out = [sem(f"right_out{s}") for s in range(YB)]

        def half(h):
            return slice(h * HALF, (h + 1) * HALF)

        block = ctx.enter_context(nc.Block())

        @block.sync
        def _(sp):
            def load_w0(r, s, always=False):
                if not always:
                    sp.wait_ge(w0_loaded[s], r * (PAIR * 16))
                for k in range(PAIR):
                    b = r * ROUND_B + (s * PAIR + k)
                    i = sp.value_load(cond0_sb[0:1, bass.ds(b, 1)], min_val=0, max_val=N0 - 1)
                    needed = None if always else sp.value_load(at_home_row[0:1, bass.ds(b, 1)], min_val=0, max_val=1)
                    sp.dma_start(w0_home[:, bass.ds(b, 1), :].rearrange("k b c -> k (b c)"),
                                 w0_t[bass.ds(i, 1), :, :].rearrange("n k c -> (n k) c"), cond=needed)\
                      .then_inc(w0_loaded[s], 16)

            def load_x(r, s):
                sp.dma_start(xy[:, s, :, :],
                             x_v[bass.ds(r * RING + s, 1), :, :, :].rearrange("n c k t -> (n c) k t"))\
                  .then_inc(x_loaded[s], 16)

            sp.dma_start(cond0_sb[:], cond0).then_inc(cond0_loaded, 16)
            for s in range(LEAD):
                load_x(0, s)
            sp.wait_ge(cond0_loaded, 16)
            for s in range(LEAD):
                load_w0(0, s, always=True)
            for s in range(LEAD, RING):
                load_w0(0, s, always=True)
                load_x(0, s)

            sp.wait_ge(home_ready, 2)
            for s in range(LEAD):
                load_w0(1, s)
            with sp.Fori(1, ROUNDS - 1) as r:
                for s in range(RING):
                    load_w0(*((r, s + LEAD) if s + LEAD < RING else (r + 1, s + LEAD - RING)))
                    sp.wait_ge(stored[s], r * 16)
                    load_x(r, s)

            for s in range(RING - 1):
                if s + LEAD < RING:
                    load_w0(ROUNDS - 1, s + LEAD)
                sp.wait_ge(stored[s], (ROUNDS - 1) * 16)
                load_x(ROUNDS - 1, s)
            sp.wait_ge(stored[LAST], (ROUNDS - 1) * 16)
            for k in range(PAIR):
                for h in range(2):
                    sp.dma_start(xy[:, LAST, k, half(h)], x[B - PAIR + k, :, half(h)])\
                      .then_inc(last_x_loaded[2 * k + h], 16)
            for k in range(PAIR):
                b = LAST * PAIR + k
                sp.wait_ge(left_out[b % YB], (ROUNDS - 1) * (ROUND_B // YB) + b // YB + 1)
                sp.dma_start(out[B - PAIR + k, :, half(0)], xy[:, LAST, k, half(0)]).then_inc(last_stored, 16)
            sp.wait_ge(last_stored, 2 * PAIR * 16)

        @block.gpsimd
        def _(pool):
            def pick(r, s):
                pool.wait_ge(w0_loaded[s], r * (PAIR * 16) + PAIR * 16)
                for k in range(PAIR):
                    b = r * ROUND_B + (s * PAIR + k)
                    home = pool.value_load(home_row[0:1, bass.ds(b, 1)], min_val=0, max_val=B - 1)
                    nc.gpsimd.tensor_copy(w0_pick[:, s, k, :],
                                          w0_home[:, bass.ds(home, 1), :].rearrange("k b c -> k (b c)"))
                    i = pool.value_load(cond1_sb[0:1, bass.ds(b, 1)], min_val=0, max_val=N1 - 1)
                    last = nc.gpsimd.tensor_copy(
                        j_pick[:, s, k, :], j_all[:, bass.ds(i, 1), :].rearrange("c n d -> c (n d)"))
                last.then_inc(picked, 1)

            nc.gpsimd.memset(eye[:], 0.0).then_inc(eye_cleared, 1)
            pool.wait_ge(eye_cleared, 1)
            nc.gpsimd.affine_select(out=eye[:], in_=eye[:], compare_op=ALU.not_equal, fill=1.0, base=0,
                                    pattern=[[-1, D]], channel_multiplier=1).then_inc(eye_ready, 1)
            nc.gpsimd.iota(batch_less_b[:], pattern=[[1, B]], base=-B, channel_multiplier=0,
                           allow_small_or_imprecise_dtypes=True).then_inc(batch_counted, 1)
            pool.wait_ge(cond1_loaded, 16)
            pool.wait_ge(home_ready, 2)
            pool.wait_ge(bias_in_j, 1)
            pool.wait_ge(j_ready, 1)
            for s in range(RING):
                pick(0, s)
            with pool.Fori(1, ROUNDS) as r:
                for s in range(RING):
                    pool.wait_ge(stored[s], r * 16)
                    pick(r, s)

        @block.tensor
        def _(pe):
            def product(r, s, first=False):
                pe.wait_ge(picked, r * RING + (s + 1))
                if not first or s >= MB:
                    pe.wait_ge(m_ready[s % MB], r * (RING // MB) + s // MB)
                for k in range(PAIR):
                    last = nc.tensor.matmul(m_ps[:, s % MB, k * D:(k + 1) * D], w0_pick[:, s, k, :],
                                            j_pick[:, s, k, 0:D], start=True, stop=True)
                last.then_inc(product_ready, 1)

            def results(r, s, k, first=False, last=False):
                b = s * PAIR + k
                if k == 0:
                    if not last:
                        pe.wait_ge(x_loaded[s], r * 16 + 16)
                    pe.wait_ge(m_ready[s % MB], r * (RING // MB) + (s // MB + 1))
                for h in range(2):
                    if last:
                        pe.wait_ge(last_x_loaded[2 * k + h], 16)
                    if not first or b >= YB:
                        pe.wait_ge((left_out, right_out)[h][b % YB], r * (ROUND_B // YB) + b // YB)
                    nc.tensor.matmul(y_ps[:, b % YB, h, :], m_sb[:, s, k, :], xy[:, s, k, half(h)],
                                     start=True, stop=True).then_inc(y_ready, 1)

            pe.wait_ge(eye_ready, 1)
            pe.wait_ge(home_step, 4)
            nc.tensor.matmul(home_ps[0:1, 0:B], home_less_b[:], eye[:], start=True, stop=True)\
              .then_inc(home_turned, 1)

            product(0, 0, first=True)
            for s in range(1, RING):
                results(0, s - 1, 0, first=True)
                product(0, s, first=True)
                results(0, s - 1, 1, first=True)
            with pe.Fori(1, ROUNDS) as r:
                results(r - 1, LAST, 0)
                product(r, 0)
                results(r - 1, LAST, 1)
                for s in range(1, RING):
                    results(r, s - 1, 0)
                    product(r, s)
                    results(r, s - 1, 1)
            for k in range(PAIR):
                results(ROUNDS - 1, LAST, k, last=True)

        @block.vector
        def _(dve):
            dve.wait_ge(cond0_compared, 32)
            nc.vector.tensor_copy(cond0_f32[:], cond0_col_sb[:]).then_inc(home_step, 1)
            dve.wait_ge(home_step, 1)
            nc.vector.tensor_scalar(same[:], cond0_rows[:], cond0_f32[:], None, ALU.is_equal).then_inc(home_step, 1)
            dve.wait_ge(home_step, 2)
            dve.wait_ge(batch_counted, 1)
            nc.vector.tensor_tensor(same_batch[:], same[:], batch_less_b[:], ALU.mult).then_inc(home_step, 1)
            dve.wait_ge(home_step, 3)
            nc.vector.tensor_reduce(home_less_b[:], same_batch[:], mybir.AxisListType.X, ALU.min)\
              .then_inc(home_step, 1)
            dve.wait_ge(home_turned, 1)
            nc.vector.tensor_scalar(home_row[:], home_ps[0:1, 0:B], float(B), None, ALU.add).then_inc(home_ready, 1)
            nc.vector.tensor_tensor(at_home_row[:], home_ps[0:1, 0:B], batch_less_b[0:1, :], ALU.is_equal)\
              .then_inc(home_ready, 1)

            dve.wait_ge(bias_loaded, 16)
            nc.vector.tensor_copy(j_all[:, :, D:D + 1], bias_sb[:].rearrange("d (n o) -> d n o", o=1))\
              .then_inc(bias_in_j, 1)
            dve.wait_ge(w1_loaded, 16)
            dve.wait_ge(eye_ready, 1)
            for n in range(N1):
                last = nc.vector.tensor_tensor(j_all[:, n, 0:D], w1_sb[:, n, :], eye[:], ALU.add)
            last.then_inc(j_ready, 1)

            def sum_m(r, s):
                dve.wait_ge(picked, r * RING + (s + 1))
                dve.wait_ge(product_ready, r * RING + (s + 1))
                nc.vector.tensor_tensor(m_sb[:, s, :, :],
                                        m_ps[:, s % MB, 0:PAIR * D].rearrange("c (k d) -> c k d", k=PAIR),
                                        j_pick[:, s, :, 0:D], ALU.add).then_inc(m_ready[s % MB], 1)

            def left(r, s, k):
                b = s * PAIR + k
                dve.wait_ge(y_ready, r * (2 * ROUND_B) + (2 * b + 1))
                nc.vector.tensor_scalar(xy[:, s, k, half(0)], y_ps[:, b % YB, 0, :], j_pick[:, s, k, D:D + 1], None,
                                        ALU.add).then_inc(left_out[b % YB], 1)

            sum_m(0, 0)
            with dve.Fori(0, ROUNDS - 1) as r:
                for s in range(RING):
                    left(r, s, 0)
                    sum_m(*((r, s + 1) if s < LAST else (r + 1, 0)))
                    left(r, s, 1)
            for s in range(RING):
                left(ROUNDS - 1, s, 0)
                if s < LAST:
                    sum_m(ROUNDS - 1, s + 1)
                left(ROUNDS - 1, s, 1)

        @block.scalar
        def _(act):
            def right(r, s, k):
                b = s * PAIR + k
                if k == 0:
                    act.wait_ge(picked, r * RING + (s + 1))
                act.wait_ge(y_ready, r * (2 * ROUND_B) + (2 * b + 2))
                nc.scalar.activation(xy[:, s, k, half(1)], y_ps[:, b % YB, 1, :], ACT.Identity,
                                     bias=j_pick[:, s, k, D:D + 1]).then_inc(right_out[b % YB], 1)

            def store(r, s):
                for k in range(PAIR):
                    b = s * PAIR + k
                    act.wait_ge(left_out[b % YB], r * (ROUND_B // YB) + (b // YB + 1))
                    act.wait_ge(right_out[b % YB], r * (ROUND_B // YB) + (b // YB + 1))
                act.dma_start(out_v[bass.ds(r * RING + s, 1), :, :, :].rearrange("n c k t -> (n c) k t"),
                              xy[:, s, :, :]).then_inc(stored[s], 16)

            act.dma_start(cond0_rows[:], cond0.to_broadcast([B, B])).then_inc(cond0_compared, 16)
            act.dma_start(cond0_col_sb[:], cond0_col).then_inc(cond0_compared, 16)
            act.dma_start(cond1_sb[:], cond1).then_inc(cond1_loaded, 16)
            act.dma_start(bias_sb[:], bias_t).then_inc(bias_loaded, 16)
            act.dma_start(w1_sb[:], w1.rearrange("n c d -> c n d")).then_inc(w1_loaded, 16)
            with act.Fori(0, ROUNDS - 1) as r:
                for s in range(RING):
                    for k in range(PAIR):
                        right(r, s, k)
                    store(r, s)
            for s in range(RING - 1):
                for k in range(PAIR):
                    right(ROUNDS - 1, s, k)
                store(ROUNDS - 1, s)
            for k in range(PAIR):
                b = LAST * PAIR + k
                right(ROUNDS - 1, LAST, k)
                act.wait_ge(right_out[b % YB], (ROUNDS - 1) * (ROUND_B // YB) + b // YB + 1)
                act.dma_start(out[B - PAIR + k, :, half(1)], xy[:, LAST, k, half(1)]).then_inc(last_stored, 16)
            for s in range(RING):
                act.wait_ge(stored[s], (ROUNDS if s < LAST else ROUNDS - 1) * 16)


def kernel(x, itok_B_1_198, itok_B_0_7, fside_8xS_0, L0_cond_weights, L1_cond_weights):
    import numpy as np
    import concourse.bacc as bacc
    from concourse.bass_utils import run_bass_kernel_spmd

    nc = bacc.Bacc("TRN2", target_bir_lowering=False, num_devices=1)
    x = np.ascontiguousarray(x)
    arrays = {
        "x": x,
        "cond0": np.ascontiguousarray(itok_B_1_198).reshape(1, -1),
        "cond0_col": np.ascontiguousarray(itok_B_1_198).reshape(-1, 1),
        "cond1": np.ascontiguousarray(itok_B_0_7).reshape(1, -1),
        "bias_t": np.ascontiguousarray(np.asarray(fside_8xS_0).T),
        "w0_t": np.ascontiguousarray(np.asarray(L0_cond_weights).transpose(0, 2, 1)),
        "w1": np.ascontiguousarray(L1_cond_weights),
    }
    aps = [nc.dram_tensor(name, a.shape, mybir.dt.from_np(a.dtype), kind="ExternalInput").ap()
           for name, a in arrays.items()]
    out = nc.dram_tensor("out", x.shape, mybir.dt.from_np(x.dtype), kind="ExternalOutput").ap()
    conditioned_residual_kernel(nc, *aps, out)
    result = run_bass_kernel_spmd(nc, [arrays], core_ids=[0])
    return result.results[0]["out"]
```
